# Optimizing a Trainium2 kernel written in Bass

```python
import numpy as np
import jax
import jax.numpy as jnp

def _softmax(x, axis=-1):
    return jax.nn.softmax(x, axis=axis)

def _gelu(x):
    return jax.nn.gelu(x, approximate=True)

def _silu(x):
    return jax.nn.silu(x)

def _sigmoid(x):
    return jax.nn.sigmoid(x)

def _layernorm(x, axis=-1, eps=1e-05):
    m = jnp.mean(x, axis=axis, keepdims=True)
    v = jnp.var(x, axis=axis, keepdims=True)
    return (x - m) / jnp.sqrt(v + eps)

def _scatter_add(tgt, idx, src, axis=0):
    return tgt.at[idx].add(src)

def _segment_sum(src, seg, n):
    return jax.ops.segment_sum(src, seg, n)
kernel_name = 'mk_conv_preact_d2_conv_nchw256_r4_3fde74'

def setup_inputs(seed: int=0):
    np.random.seed(seed)
    _w = jnp.asarray

    def _rec_inputs():
        import jax
        import jax.numpy as jnp
        _gk = jax.random.key(seed)
        x = -0.0002091 + 1 * jax.random.normal(jax.random.fold_in(_gk, 1), (32, 64, 56, 56), jnp.float32)
        return x
    x = _rec_inputs()

    def _L0_conv_setup():
        import jax, jax.numpy as jnp
        import numpy as np
        from jax import lax
        EPS = 1e-05
        NEG_SLOPE = 0.01

        @jax.custom_vjp
        def bin_active(x):
            return jnp.sign(x)

        def _ba_fwd(x):
            return (jnp.sign(x), x)

        def _ba_bwd(x, g):
            scale = jnp.where((x >= 1.0) | (x <= -1.0), 0.01, 1.0)
            return (g * scale,)
        bin_active.defvjp(_ba_fwd, _ba_bwd)

        def channel_shuffle(x, groups=2):
            n, c, h, w = x.shape
            x = x.reshape(n, groups, c // groups, h, w)
            x = jnp.swapaxes(x, 1, 2)
            return x.reshape(n, c, h, w)

        def gconv3x3(x, w, stride=1, groups=2):
            return lax.conv_general_dilated(x, w, window_strides=(stride, stride), padding=((1, 1), (1, 1)), feature_group_count=groups, dimension_numbers=('NCHW', 'OIHW', 'NCHW'))

        def batchnorm_train(x, gamma, beta):
            mean = jnp.mean(x, axis=(0, 2, 3), keepdims=True)
            var = jnp.var(x, axis=(0, 2, 3), keepdims=True)
            xn = (x - mean) * lax.rsqrt(var + EPS)
            return xn * gamma[None, :, None, None] + beta[None, :, None, None]

        def leaky_relu(x):
            return jnp.where(x >= 0, x, NEG_SLOPE * x)
        key = jax.random.key(seed)
        ks = jax.random.split(key, 3)
        in_planes, planes = (64, 32)
        x = jax.random.normal(ks[0], (32, in_planes, 56, 56), dtype=jnp.float32)
        w1 = jax.random.normal(ks[1], (planes, in_planes // 2, 3, 3), dtype=jnp.float32) * 0.05
        w2 = jax.random.normal(ks[2], (planes, 2 * planes // 2, 3, 3), dtype=jnp.float32) * 0.05
        g1 = jnp.ones((planes,), jnp.float32)
        b1 = jnp.zeros((planes,), jnp.float32)
        g2 = jnp.ones((2 * planes,), jnp.float32)
        b2 = jnp.zeros((2 * planes,), jnp.float32)
        g3 = jnp.ones((planes,), jnp.float32)
        b3 = jnp.zeros((planes,), jnp.float32)
        return {'x': x, 'w1': w1, 'w2': w2, 'g1': g1, 'b1': b1, 'g2': g2, 'b2': b2, 'g3': g3, 'b3': b3}
    _L0_conv_all = _L0_conv_setup()
    _L0_conv_in = {k: v for k, v in _L0_conv_all.items() if k in ('w1', 'w2', 'g1', 'b1', 'g2', 'b2', 'g3', 'b3')}
    del _L0_conv_all

    def _L1_conv_setup():
        import jax, jax.numpy as jnp
        import numpy as np
        C = 64
        G = 8
        K = 9
        DWK = 3
        OFFSET_SCALE = 1.0
        N, H, W = (8, 16, 16)
        key = jax.random.key(seed)
        ks = jax.random.split(key, 6)

        def init(k, shape, fan):
            return jax.random.normal(k, shape, jnp.float32) * fan ** (-0.5)
        return {'x': jax.random.normal(ks[0], (N, C, H, W), jnp.float32), 'dw_w': init(ks[1], (C, 1, DWK, DWK), DWK * DWK), 'dw_b': jnp.zeros((C,), jnp.float32), 'om_w': init(ks[2], (G * K * 3, C), C) * 0.01, 'om_b': jnp.zeros((G * K * 3,), jnp.float32), 'vp_w': init(ks[3], (C, C), C), 'vp_b': jnp.zeros((C,), jnp.float32), 'op_w': init(ks[4], (C, C), C)}
    _L1_conv_all = _L1_conv_setup()
    _L1_conv_in = {k: v for k, v in _L1_conv_all.items() if k in ('dw_w', 'dw_b', 'om_w', 'om_b', 'vp_w', 'vp_b', 'op_w')}
    del _L1_conv_all
    return {'x': x, 'L0_conv_w1': _L0_conv_in['w1'], 'L0_conv_w2': _L0_conv_in['w2'], 'L0_conv_g1': _L0_conv_in['g1'], 'L0_conv_b1': _L0_conv_in['b1'], 'L0_conv_g2': _L0_conv_in['g2'], 'L0_conv_b2': _L0_conv_in['b2'], 'L0_conv_g3': _L0_conv_in['g3'], 'L0_conv_b3': _L0_conv_in['b3'], 'L1_conv_dw_w': _L1_conv_in['dw_w'], 'L1_conv_dw_b': _L1_conv_in['dw_b'], 'L1_conv_om_w': _L1_conv_in['om_w'], 'L1_conv_om_b': _L1_conv_in['om_b'], 'L1_conv_vp_w': _L1_conv_in['vp_w'], 'L1_conv_vp_b': _L1_conv_in['vp_b'], 'L1_conv_op_w': _L1_conv_in['op_w']}

def reference(x, L0_conv_w1, L0_conv_w2, L0_conv_g1, L0_conv_b1, L0_conv_g2, L0_conv_b2, L0_conv_g3, L0_conv_b3, L1_conv_dw_w, L1_conv_dw_b, L1_conv_om_w, L1_conv_om_b, L1_conv_vp_w, L1_conv_vp_b, L1_conv_op_w):
    import jax
    import jax.numpy as jnp

    def _L0_conv_ref(x, w1, w2, g1, b1, g2, b2, g3, b3):
        import jax, jax.numpy as jnp
        import numpy as np
        from jax import lax
        EPS = 1e-05
        NEG_SLOPE = 0.01

        @jax.custom_vjp
        def bin_active(x):
            return jnp.sign(x)

        def _ba_fwd(x):
            return (jnp.sign(x), x)

        def _ba_bwd(x, g):
            scale = jnp.where((x >= 1.0) | (x <= -1.0), 0.01, 1.0)
            return (g * scale,)
        bin_active.defvjp(_ba_fwd, _ba_bwd)

        def channel_shuffle(x, groups=2):
            n, c, h, w = x.shape
            x = x.reshape(n, groups, c // groups, h, w)
            x = jnp.swapaxes(x, 1, 2)
            return x.reshape(n, c, h, w)

        def gconv3x3(x, w, stride=1, groups=2):
            return lax.conv_general_dilated(x, w, window_strides=(stride, stride), padding=((1, 1), (1, 1)), feature_group_count=groups, dimension_numbers=('NCHW', 'OIHW', 'NCHW'))

        def batchnorm_train(x, gamma, beta):
            mean = jnp.mean(x, axis=(0, 2, 3), keepdims=True)
            var = jnp.var(x, axis=(0, 2, 3), keepdims=True)
            xn = (x - mean) * lax.rsqrt(var + EPS)
            return xn * gamma[None, :, None, None] + beta[None, :, None, None]

        def leaky_relu(x):
            return jnp.where(x >= 0, x, NEG_SLOPE * x)
        x = channel_shuffle(x, 2)
        xa, xb = jnp.split(x, 2, axis=1)
        x1 = bin_active(x)
        x1 = gconv3x3(x1, w1, stride=1, groups=2)
        x1 = leaky_relu(x1)
        x2 = batchnorm_train(x1, g1, b1)
        x3 = jnp.concatenate((x2 + xa, xb), axis=1)
        x3 = batchnorm_train(x3, g2, b2)
        x3 = channel_shuffle(x3, 2)
        x4 = bin_active(x3)
        x4 = gconv3x3(x4, w2, stride=1, groups=2)
        x4 = leaky_relu(x4)
        x4 = batchnorm_train(x4, g3, b3)
        x5a, x5b = jnp.split(x3, 2, axis=1)
        return jnp.concatenate((x4 + x5a, x5b), axis=1)

    def _L1_conv_ref(x, dw_w, dw_b, om_w, om_b, vp_w, vp_b, op_w):
        import jax, jax.numpy as jnp
        import numpy as np
        C = 64
        G = 8
        K = 9
        DWK = 3
        OFFSET_SCALE = 1.0
        N, H, W = (8, 16, 16)
        n, c, h, w = x.shape
        cg = c // G
        L = h * w
        xf = x.transpose(0, 2, 3, 1).reshape(n, L, c)
        value = (xf @ vp_w.T + vp_b).reshape(n, L, G, cg)
        om_in = jax.lax.conv_general_dilated(x, dw_w, (1, 1), 'SAME', feature_group_count=c, dimension_numbers=('NCHW', 'OIHW', 'NCHW')) + dw_b[None, :, None, None]
        om = om_in.transpose(0, 2, 3, 1).reshape(n, L, c) @ om_w.T + om_b
        om = om.reshape(n, h, w, G, K * 3)
        off = om[..., :2 * K].reshape(n, h, w, G, K, 2) * OFFSET_SCALE
        mask = om[..., 2 * K:]
        d = jnp.arange(-1, 2, dtype=jnp.float32)
        dy, dx = jnp.meshgrid(d, d, indexing='ij')
        base = jnp.stack([dy.ravel(), dx.ravel()], -1)
        py = jnp.arange(h, dtype=jnp.float32).reshape(1, h, 1, 1, 1) + base[:, 0].reshape(1, 1, 1, 1, K) + off[..., 0]
        px = jnp.arange(w, dtype=jnp.float32).reshape(1, 1, w, 1, 1) + base[:, 1].reshape(1, 1, 1, 1, K) + off[..., 1]
        y0 = jnp.floor(py)
        x0 = jnp.floor(px)
        ty = py - y0
        tx = px - x0
        y0i = y0.astype(jnp.int32)
        x0i = x0.astype(jnp.int32)

        def gather(yi, xi, wgt):
            valid = (yi >= 0) & (yi < h) & (xi >= 0) & (xi < w)
            idx = jnp.clip(yi, 0, h - 1) * w + jnp.clip(xi, 0, w - 1)
            idx = idx.transpose(0, 1, 2, 4, 3).reshape(n, L * K, G)[..., None]
            g = jnp.take_along_axis(value, idx, axis=1)
            g = g.reshape(n, h, w, K, G, cg).transpose(0, 1, 2, 4, 3, 5)
            return g * (wgt * valid)[..., None]
        sampled = gather(y0i, x0i, (1 - ty) * (1 - tx)) + gather(y0i, x0i + 1, (1 - ty) * tx) + gather(y0i + 1, x0i, ty * (1 - tx)) + gather(y0i + 1, x0i + 1, ty * tx)
        out = jnp.einsum('nhwgk,nhwgkc->nhwgc', mask, sampled)
        out = out.reshape(n, L, c) @ op_w.T
        return out.reshape(n, h, w, c).transpose(0, 3, 1, 2)

    def _gn(v, G=32, eps=1e-05):
        B_, C_, H_, W_ = v.shape
        g = v.reshape(B_, G, C_ // G, H_, W_)
        m = jnp.mean(g, axis=(2, 3, 4), keepdims=True)
        s = jnp.var(g, axis=(2, 3, 4), keepdims=True)
        return ((g - m) / jnp.sqrt(s + eps)).reshape(v.shape)

    def _ln_c(v, eps=1e-06):
        m = jnp.mean(v, axis=1, keepdims=True)
        s = jnp.var(v, axis=1, keepdims=True)
        return (v - m) / jnp.sqrt(s + eps)

    def _ln_t(v, eps=1e-05):
        m = jnp.mean(v, axis=-1, keepdims=True)
        s = jnp.var(v, axis=-1, keepdims=True)
        return (v - m) / jnp.sqrt(s + eps)

    def _to_tokens(v):
        B_, C_, H_, W_ = v.shape
        return v.reshape(B_, C_, H_ * W_).transpose(0, 2, 1)

    def _from_tokens(t, like):
        B_, C_, H_, W_ = like.shape
        return t.transpose(0, 2, 1).reshape(B_, C_, H_, W_)
    x = x + _L0_conv_ref(_gn(x), L0_conv_w1, L0_conv_w2, L0_conv_g1, L0_conv_b1, L0_conv_g2, L0_conv_b2, L0_conv_g3, L0_conv_b3)
    x = x + _L1_conv_ref(_gn(x), L1_conv_dw_w, L1_conv_dw_b, L1_conv_om_w, L1_conv_om_b, L1_conv_vp_w, L1_conv_vp_b, L1_conv_op_w)
    return x

_drawn_inputs = setup_inputs


def setup_inputs(seed=0):
    import zlib

    import numpy as np

    out = dict(_drawn_inputs(seed))
    spreads = {'L0_conv_g1': (1.0, 0.2),
     'L0_conv_b1': (0.0, 0.8),
     'L0_conv_g2': (1.0, 0.2),
     'L0_conv_b2': (0.0, 0.1),
     'L0_conv_g3': (1.0, 0.2),
     'L0_conv_b3': (0.0, 0.1),
     'L1_conv_dw_b': (0.0, 0.8),
     'L1_conv_om_b': (0.0, 0.1),
     'L1_conv_vp_b': (0.0, 0.637)}
    factors = {'L1_conv_dw_w': 3.491, 'L1_conv_om_w': 3.482}
    for name, (base, spread) in spreads.items():
        noise = np.random.default_rng([zlib.crc32(name.encode()), seed]).standard_normal(out[name].shape)
        drawn = base * np.exp(spread * noise) if base else spread * noise
        out[name] = jnp.asarray(drawn.astype(out[name].dtype))
    for name, factor in factors.items():
        out[name] = (out[name] * factor).astype(out[name].dtype)
    return out
```

```python
from contextlib import ExitStack

import numpy as np
import concourse.bass as bass
from concourse import mybir

f32 = mybir.dt.float32
i32 = mybir.dt.int32
bf16 = mybir.dt.bfloat16
ALU = mybir.AluOpType
ACT = mybir.ActivationFunctionType
AX = mybir.AxisListType

H = W = 56
HW = H * W
C = 64
CO = 32
S = 2
HH = H // 2
HALF = HH * W
TAPS = 9
PARTS = 3
CR = 7
NCH = HH // CR
CN = CR * W
PW = W + 2
NXB = 3
EPS = 1e-5
SLOPE = 0.01
BN_F = 6
G = 8
GK = G * TAPS
OMC = 3 * GK
LANES = 2 * PW
BR = 4
NBLK = HH // BR
RP = BR // 2
GK2 = 2 * GK
WIN = 5
SLOTS = 5
VR = 8
DR = 2
PIECES = 4
PIECE = HW // PIECES
BN3 = 448
BANK = 512
TP = 2 * W
TILES = HW // TP
VP = W + 5
W3 = OMC + 3 * C + TAPS + 1
G1, B1, G2A, G2B, B2A, B2B, G3, B3 = range(8)


def wait(eng, sem, value):
    if not isinstance(value, int) or value > 0:
        eng.wait_ge(sem, value)


def l0_passes(nc, x, w1t, w2t, par, con, l1_d, l2_d, x3_d, ab3, pairs):
    ctx = ExitStack()
    with ctx:
        def sb(name, shape, dt=f32):
            return ctx.enter_context(nc.sbuf_tensor(name, shape, dt))

        def sem(name):
            return ctx.enter_context(nc.semaphore(name))

        wf = sb("wf", [128, TAPS, S * CO])
        wr = sb("wr", [128, TAPS, S * CO])
        wb = sb("wb", [128, 2, PARTS, TAPS, S * CO], bf16)
        prm = sb("prm", [128, 8])
        avg = sb("avg", [128, 3, 128])
        xt = sb("xt", [128, NXB, 2, HALF])
        lt = sb("lt", [128, 2, HALF])
        lin = sb("lin", [128, 2, HALF])
        sg = sb("sg", [128, 2, 2, HH, PW], bf16)
        cin = sb("cin", [128, 2, H + 2, PW], bf16)
        junk = sb("junk", [128, HALF])
        bx = sb("bx", [128, 2, NCH, BN_F])
        mv = sb("mv", [128, 2, 2])
        rhs = sb("rhs", [128, 2, 2])
        gs = sb("gs", [128, 2, 4, 2])
        eps = sb("eps", [128, 2])
        spare = sb("spare", [128, 1])
        half = sb("half", [128, 2])
        cross = sb("cross", [128, 2])
        st_c = sb("st_c", [128, pairs, 2, 2])
        st_g = sb("st_g", [128, pairs, 4, 2])
        st_x = sb("st_x", [128, pairs])
        st_l = sb("st_l", [128, pairs, NCH, BN_F])
        sc = sb("sc", [128, 40])
        vv = sb("vv", [128, 8, pairs])
        aff = sb("aff", [128, pairs, 4])
        af = sb("af", [128, 2, 4])
        cv = [ctx.enter_context(nc.psum_tensor(f"cv{c}", [128, 512], f32)) for c in range(NCH)]
        ps = ctx.enter_context(nc.psum_tensor("ps", [128, 512], f32))

        NX = 4 * 16
        NS = 4 * 16

        def buf(p):
            return bass.ts(p % NXB, 1)

        def load_x(eng, p, done):
            for h in range(2):
                for s in range(S):
                    at = 64 * h + CO * s
                    eng.dma_start(
                        xt[at:at + CO, buf(p), :, :].rearrange("p a t f -> p (a t) f"),
                        x[S * p + s, :, h * HALF:(h + 1) * HALF].rearrange("(g t c) f -> c g t f", g=2, t=2),
                    ).then_inc(done, 16)

        def x_of(p, t):
            return xt[:, buf(p), t, :].rearrange("p a f -> p (a f)")

        def rows(ap):
            return ap.rearrange("p (r w) -> p r w", w=W)

        def settle(eng):
            eng.wait_ge(par_in, 32)

        def move_signs(eng, u, done):
            for t in range(2):
                for h in range(2):
                    eng.dma_start(cin[64 * t:64 * t + 64, u, 1 + HH * h:1 + HH * (h + 1), :],
                                  sg[64 * h:64 * h + 64, u, t, :, :]).then_inc(done, 16)

        def conv_chunk(pe, layer, u, c, done):
            for k in range(TAPS):
                for j in range(PARTS):
                    for h in range(2):
                        r = HH * h + CR * c + k // 3
                        mm = pe.matmul(cv[c][64 * h:64 * h + 64, 0:CN], wb[:, layer, j, k, :],
                                       cin[:, u, r:r + CR, k % 3:k % 3 + W],
                                       start=(k == 0 and j == 0), stop=(k == TAPS - 1 and j == PARTS - 1))
            mm.then_inc(done, 1)

        def evacuate(act, u, c, conv, conv_at, done):
            act.wait_ge(conv, conv_at)
            act.activation(lt[:, u, CN * c:CN * (c + 1)], cv[c][:, 0:CN], ACT.Copy).then_inc(done, 1)

        def steps(eng, done):
            n = [0]

            def then(ins):
                n[0] += 1
                ins.then_inc(done, 1)
                eng.wait_ge(done, n[0])
            return then

        par_in, w_in, w_zero, w_split, cleared = map(sem, ("par_in", "w_in", "w_zero", "w_split", "cleared"))
        with nc.Block() as block:
            @block.sync
            def _(sp):
                sp.dma_start(prm[:, :], par).then_inc(par_in, 16)
                sp.dma_start(avg[:, :, :], con).then_inc(par_in, 16)
                sp.wait_ge(w_zero, 1)
                for t in range(2):
                    for s in range(S):
                        at, oc = 64 * t + CO * s, CO * s + 16 * t
                        sp.dma_start(wf[at:at + CO, :, oc:oc + 16], w1t[:, :, 16 * t:16 * t + 16]).then_inc(w_in, 16)
                sp.wait_ge(w_zero, 2)
                for t in range(2):
                    for s in range(S):
                        for q in range(2):
                            at = 64 * t + CO * s + 16 * q
                            oc = CO * s + 16 * q
                            sp.dma_start(wf[at:at + 16, :, oc:oc + 16],
                                         w2t[t, :, :, 16 * q:16 * q + 16]).then_inc(w_in, 16)
                sp.wait_ge(par_in, 32)

            @block.gpsimd
            def _(pool):
                for col in (0, PW - 1):
                    pool.memset(sg[:, :, :, :, col:col + 1], 0.0)
                for row in (0, H + 1):
                    pool.memset(cin[:, :, row, :], 0.0)
                pool.memset(eps[:, :], EPS)
                pool.memset(half[:, :], -0.5).then_inc(cleared, 1)
                pool.wait_ge(cleared, 1)

            @block.vector
            def _(dve):
                then = steps(dve, w_split)
                for layer, loads in ((0, 4), (1, 12)):
                    dve.memset(wf[:, :, :], 0.0).then_inc(w_zero, 1)
                    dve.wait_ge(w_in, 16 * loads)
                    then(dve.tensor_copy(wb[:, layer, 0], wf[:, :, :]))
                    then(dve.tensor_tensor(wr[:, :, :], wf[:, :, :], wb[:, layer, 0], ALU.subtract))
                    then(dve.tensor_copy(wb[:, layer, 1], wr[:, :, :]))
                    then(dve.tensor_tensor(wr[:, :, :], wr[:, :, :], wb[:, layer, 1], ALU.subtract))
                    then(dve.tensor_copy(wb[:, layer, 2], wr[:, :, :]))

        x_in = [sem("x_in0"), sem("x_in1")]
        signs_in = [sem("signs_in0"), sem("signs_in1")]
        l1_out = [sem("l1_out0"), sem("l1_out1")]
        bx_ok, mv_ok, sq_ok, rhs_ok, grp_ok, neg_ok, m2_ok, var_ok, eps_ok, rstd_ok, sign_ok = map(sem, (
            "bx_ok", "mv_ok", "sq_ok", "rhs_ok", "grp_ok", "neg_ok", "m2_ok", "var_ok", "eps_ok", "rstd_ok", "sign_ok"))
        conv_ok, evac_ok, leaky_ok, cross_ok, used_ok = map(sem, ("conv_ok", "evac_ok", "leaky_ok", "cross_ok", "used_ok"))
        with nc.Block() as block:
            @block.sync
            def _(sp):
                def signs(p, u):
                    sp.wait_ge(sign_ok, p + 1)
                    move_signs(sp, u, signs_in[u])

                def step(p, u, last):
                    if not last:
                        signs(p + 1, 1 - u)
                    sp.wait_ge(leaky_ok, p + 1)
                    sp.dma_start(l1_d[p, :, :], lt[:, u, :]).then_inc(l1_out[u], 16)

                load_x(sp, 0, x_in[0])
                load_x(sp, 1, x_in[1])
                sp.wait_ge(x_in[0], NX)
                load_x(sp, 2, x_in[0])
                signs(0, 0)
                with sp.Fori(0, pairs // 2 - 2) as i:
                    for u in range(2):
                        step(2 * i + u, u, False)
                        settle(sp)
                        sp.wait_ge(used_ok, 2 * i + u + 1)
                        load_x(sp, 2 * i + u + 3, x_in[1 - u])
                step(pairs - 4, 0, False)
                sp.wait_ge(used_ok, pairs - 3)
                load_x(sp, pairs - 1, x_in[1])
                step(pairs - 3, 1, False)
                step(pairs - 2, 0, False)
                step(pairs - 1, 1, True)
                for u in range(2):
                    sp.wait_ge(l1_out[u], 16 * (pairs // 2))

            @block.vector
            def _(dve):
                def channel_stats(p, i, u):
                    dve.wait_ge(x_in[u], NX * i + NX)
                    for t in range(2):
                        for c in range(NCH):
                            b = dve.bn_stats(bx[:, t, c, :], x_of(p, t)[:, CN * c:CN * (c + 1)])
                    b.then_inc(bx_ok, 1)
                    dve.wait_ge(bx_ok, p + 1)
                    dve.tensor_copy(spare[:, :], bx[:, 0, 0, 0:1])
                    for t in range(2):
                        b = dve.bn_aggr(mv[:, t, :], bx[:, t, :, :].rearrange("p c f -> p (c f)"))
                    b.then_inc(mv_ok, 1)
                    dve.wait_ge(mv_ok, p + 1)
                    dve.tensor_copy(rhs[:, :, 0], mv[:, :, 0])
                    dve.tensor_tensor(rhs[:, :, 1], mv[:, :, 0], mv[:, :, 0], ALU.mult).then_inc(sq_ok, 1)
                    dve.wait_ge(sq_ok, p + 1)
                    dve.tensor_tensor(rhs[:, :, 1], rhs[:, :, 1], mv[:, :, 1], ALU.add).then_inc(rhs_ok, 1)

                def group_stats(p, u):
                    gp = ps[:, 0:4].rearrange("p (t k) -> p t k", t=2)
                    dve.wait_ge(grp_ok, p + 1)
                    dve.tensor_copy(st_c[:, bass.ts(p, 1), :, :].rearrange("p a t k -> p (a t) k"), rhs[:, :, :])
                    dve.tensor_copy(gs[:, u, 0, :], gp[:, :, 0])
                    dve.tensor_scalar(gs[:, u, 3, :], gp[:, :, 0], -1.0, None, ALU.mult).then_inc(neg_ok, 1)
                    dve.wait_ge(neg_ok, p + 1)
                    dve.tensor_tensor(gs[:, u, 1, :], gs[:, u, 0, :], gs[:, u, 3, :], ALU.mult).then_inc(m2_ok, 1)
                    dve.wait_ge(m2_ok, p + 1)
                    dve.tensor_tensor(gs[:, u, 1, :], gs[:, u, 1, :], gp[:, :, 1], ALU.add).then_inc(var_ok, 1)

                def leaky(p, u):
                    dve.wait_ge(evac_ok, NCH * (p + 1))
                    dve.scalar_tensor_tensor(out=lt[:, u, :], in0=lt[:, u, :], scalar=SLOPE, in1=lt[:, u, :],
                                             op0=ALU.mult, op1=ALU.max).then_inc(leaky_ok, 1)

                def moments(p, u):
                    dve.wait_ge(leaky_ok, p + 1)
                    for c in range(NCH):
                        dve.bn_stats(st_l[:, bass.ts(p, 1), c, :].rearrange("p a f -> p (a f)"),
                                     lt[:, u, CN * c:CN * (c + 1)])
                    dve.scalar_tensor_tensor(out=junk[:, :], in0=x_of(p, 0), scalar=gs[:, u, 0, 0:1],
                                             in1=lt[:, u, :], op0=ALU.subtract, op1=ALU.mult,
                                             accum_out=cross[:, u:u + 1]).then_inc(cross_ok, 1)
                    dve.wait_ge(rstd_ok, p + 1)
                    dve.tensor_copy(st_g[:, bass.ts(p, 1), :, :].rearrange("p a k t -> p (a k) t"), gs[:, u, :, :])
                    dve.wait_ge(cross_ok, p + 1)
                    dve.tensor_copy(st_x[:, bass.ts(p, 1)], cross[:, u:u + 1]).then_inc(used_ok, 1)
                    dve.wait_ge(used_ok, p + 1)

                def step(p, i, u, last):
                    if not last:
                        channel_stats(p + 1, i + u, 1 - u)
                        group_stats(p + 1, 1 - u)
                    leaky(p, u)
                    moments(p, u)

                channel_stats(0, 0, 0)
                group_stats(0, 0)
                with dve.Fori(0, pairs // 2 - 1) as i:
                    for u in range(2):
                        step(2 * i + u, i, u, False)
                step(pairs - 2, pairs // 2 - 1, 0, False)
                step(pairs - 1, pairs // 2 - 1, 1, True)

            @block.gpsimd
            def _(pool):
                def rstd(p, u):
                    pool.wait_ge(var_ok, p + 1)
                    pool.tensor_tensor(gs[:, u, 2, :], gs[:, u, 1, :], eps[:, :], ALU.add).then_inc(eps_ok, 1)
                    pool.wait_ge(eps_ok, p + 1)
                    pool.tensor_tensor(gs[:, u, 2, :], gs[:, u, 2, :], half[:, :], ALU.pow).then_inc(rstd_ok, 1)

                with pool.Fori(0, pairs // 2) as i:
                    for u in range(2):
                        rstd(2 * i + u, u)

            @block.scalar
            def _(act):
                def signs(p, i, u):
                    act.wait_ge(neg_ok, p + 1)
                    wait(act, signs_in[u], NS * i)
                    for t in range(2):
                        a = act.activation(sg[:, u, t, :, 1:1 + W],
                                           rows(x_of(p, t)),
                                           ACT.Sign, bias=gs[:, u, 3, t:t + 1])
                    a.then_inc(sign_ok, 1)

                def step(p, i, u, last):
                    wait(act, l1_out[u], 16 * i)
                    for c in range(NCH):
                        if c == 2 and not last:
                            signs(p + 1, i + u, 1 - u)
                        evacuate(act, u, c, conv_ok, NCH * p + c + 1, evac_ok)

                signs(0, 0, 0)
                with act.Fori(0, pairs // 2 - 1) as i:
                    for u in range(2):
                        step(2 * i + u, i, u, False)
                step(pairs - 2, pairs // 2 - 1, 0, False)
                step(pairs - 1, pairs // 2 - 1, 1, True)

            @block.tensor
            def _(pe):
                def groups(p):
                    pe.wait_ge(rhs_ok, p + 1)
                    wait(pe, var_ok, p)
                    pe.matmul(ps[:, 0:4], avg[:, 0, :], rhs[:, :, :], start=True, stop=True).then_inc(grp_ok, 1)

                def step(p, i, u, last):
                    pe.wait_ge(signs_in[u], NS * i + NS)
                    for c in range(NCH):
                        if c == 2 and not last:
                            groups(p + 1)
                        wait(pe, evac_ok, NCH * (p - 1) + c + 1)
                        conv_chunk(pe, 0, u, c, conv_ok)

                groups(0)
                step(0, 0, 0, False)
                step(1, 0, 1, False)
                with pe.Fori(1, pairs // 2 - 1) as i:
                    for u in range(2):
                        step(2 * i + u, i, u, False)
                step(pairs - 2, pairs // 2 - 1, 0, False)
                step(pairs - 1, pairs // 2 - 1, 1, True)

        fold, avg_ok, bvar_ok, beps_ok, brstd_ok = map(sem, ("fold", "avg_ok", "bvar_ok", "beps_ok", "brstd_ok"))
        ML, EL, MA, EA, ELA, MB, EB = range(7)
        AV = 8
        V1, COV, V2A, V2B, R1, R2A, R2B, SCA, SCB, A1, T0, T1, KA, KB, ALPHA = range(16, 31)
        with nc.Block() as block:
            @block.vector
            def _(dve):
                then = steps(dve, fold)
                c = lambda n: sc[:, n:n + 1]
                m = lambda n: sc[:, AV + n:AV + n + 1]
                q = lambda n: prm[:, n:n + 1]

                def tt(out, a, b, op):
                    then(dve.tensor_tensor(out, a, b, op))

                def ts(out, a, s1, s2, op0, op1=ALU.bypass):
                    then(dve.tensor_scalar(out, a, s1, s2, op0, op1))

                then(dve.bn_aggr(mv[:, 0, :], st_l[:, :, :, :].rearrange("p a c f -> p (a c f)")))
                then(dve.tensor_copy(c(ML), mv[:, 0, 0:1]))
                tt(c(EL), c(ML), c(ML), ALU.mult)
                tt(c(EL), c(EL), mv[:, 0, 1:2], ALU.add)
                for t, mean, square in ((0, MA, EA), (1, MB, EB)):
                    cm, ce = st_c[:, :, t, 0], st_c[:, :, t, 1]
                    gm, gr = st_g[:, :, 0, t], st_g[:, :, 2, t]
                    tt(vv[:, 0, :], cm, gm, ALU.subtract)
                    tt(vv[:, 0, :], vv[:, 0, :], gr, ALU.mult)
                    ts(vv[:, 1, :], cm, -2.0, None, ALU.mult)
                    tt(vv[:, 1, :], vv[:, 1, :], gm, ALU.add)
                    tt(vv[:, 1, :], vv[:, 1, :], gm, ALU.mult)
                    tt(vv[:, 1, :], vv[:, 1, :], ce, ALU.add)
                    tt(vv[:, 1, :], vv[:, 1, :], gr, ALU.mult)
                    tt(vv[:, 1, :], vv[:, 1, :], gr, ALU.mult)
                    then(dve.tensor_reduce(c(mean), vv[:, 0, :], AX.X, ALU.add))
                    then(dve.tensor_reduce(c(square), vv[:, 1, :], AX.X, ALU.add))
                    ts(c(mean), c(mean), 1.0 / pairs, None, ALU.mult)
                    ts(c(square), c(square), 1.0 / pairs, None, ALU.mult)
                tt(vv[:, 2, :], st_x[:, :], st_g[:, :, 2, 0], ALU.mult)
                then(dve.tensor_reduce(c(ELA), vv[:, 2, :], AX.X, ALU.add))
                ts(c(ELA), c(ELA), 1.0 / (pairs * HALF), None, ALU.mult)
                dve.wait_ge(avg_ok, 1)
                then(dve.tensor_copy(sc[:, AV:AV + 7], ps[:, 0:7]))
                for out, a, b, e in ((V1, ML, ML, EL), (COV, ML, MA, ELA), (V2A, MA, MA, EA), (V2B, MB, MB, EB)):
                    tt(c(T0), m(a), m(b), ALU.mult)
                    tt(c(out), m(e), c(T0), ALU.subtract)
                dve.tensor_copy(c(T1), c(V2B)).then_inc(bvar_ok, 1)
                dve.wait_ge(brstd_ok, 1)
                tt(c(A1), q(G1), c(R1), ALU.mult)
                tt(c(T0), c(A1), c(V1), ALU.mult)
                tt(c(T0), c(T0), c(COV), ALU.add)
                tt(c(T0), c(T0), c(COV), ALU.add)
                tt(c(T0), c(T0), c(A1), ALU.mult)
                tt(c(V2A), c(V2A), c(T0), ALU.add)
                dve.tensor_copy(c(T1), c(T0)).then_inc(bvar_ok, 1)
                dve.wait_ge(brstd_ok, 3)
                tt(c(SCA), q(G2A), c(R2A), ALU.mult)
                tt(c(SCB), q(G2B), c(R2B), ALU.mult)
                tt(c(ALPHA), c(A1), c(SCA), ALU.mult)
                tt(c(T0), c(A1), m(ML), ALU.mult)
                tt(c(T0), c(T0), m(MA), ALU.add)
                tt(c(T0), c(T0), c(SCA), ALU.mult)
                tt(c(KA), q(B2A), c(T0), ALU.subtract)
                tt(c(T0), m(MB), c(SCB), ALU.mult)
                tt(c(KB), q(B2B), c(T0), ALU.subtract)
                for t, scale, shift in ((0, SCA, KA), (1, SCB, KB)):
                    gm, gr = st_g[:, :, 0, t], st_g[:, :, 2, t]
                    ts(aff[:, :, 2 * t], gr, c(scale), None, ALU.mult)
                    tt(vv[:, 0, :], aff[:, :, 2 * t], gm, ALU.mult)
                    ts(aff[:, :, 2 * t + 1], vv[:, 0, :], -1.0, c(shift), ALU.mult, ALU.add)

            @block.tensor
            def _(pe):
                pe.wait_ge(fold, 4 + 2 * 12 + 3)
                pe.matmul(ps[:, 0:7], avg[:, 1, :], sc[:, 0:7], start=True, stop=True).then_inc(avg_ok, 1)

            @block.gpsimd
            def _(pool):
                def rstd(out, var):
                    pool.tensor_scalar(sc[:, out:out + 1], sc[:, var:var + 1], EPS, None, ALU.add).then_inc(beps_ok, 1)
                    n[0] += 1
                    pool.wait_ge(beps_ok, n[0])
                    pool.tensor_tensor(sc[:, out:out + 1], sc[:, out:out + 1], half[:, 0:1], ALU.pow).then_inc(brstd_ok, 1)
                n = [0]
                pool.wait_ge(bvar_ok, 1)
                rstd(R1, V1)
                rstd(R2B, V2B)
                pool.wait_ge(bvar_ok, 2)
                rstd(R2A, V2A)

        x_in2 = [sem("x_again0"), sem("x_again1")]
        l1_in = [sem("l1_in0"), sem("l1_in1")]
        signs2 = [sem("signs2_in0"), sem("signs2_in1")]
        x3_out = [sem("x3_out0"), sem("x3_out1")]
        l2_out = [sem("l2_out0"), sem("l2_out1")]
        af_ok, ta_ok, x3a_ok, x3b_ok, sign2_ok, conv2_ok, evac2_ok, leaky2_ok, stat2_ok = map(sem, (
            "af_ok", "ta_ok", "x3a_ok", "x3b_ok", "sign2_ok", "conv2_ok", "evac2_ok", "leaky2_ok", "stat2_ok"))
        NL = 2 * 16
        with nc.Block() as block:
            @block.sync
            def _(sp):
                def load_l1(p, u):
                    wait(sp, x3a_ok, p - 1)
                    sp.dma_start(lin[:, u, :], l1_d[p, :, :]).then_inc(l1_in[u], 16)

                def x3_and_signs(p, u):
                    sp.wait_ge(sign2_ok, p + 1)
                    move_signs(sp, u, signs2[u])
                    for h in range(2):
                        for s in range(S):
                            at = 64 * h + CO * s
                            sp.dma_start(
                                x3_d[S * p + s, :, h * HALF:(h + 1) * HALF].rearrange("(o t) f -> o t f", t=2),
                                xt[at:at + CO, buf(p), :, :].rearrange("p a t f -> p (a t) f")).then_inc(x3_out[u], 16)

                def step(p, u, last):
                    if not last:
                        x3_and_signs(p + 1, 1 - u)
                    sp.wait_ge(leaky2_ok, p + 1)
                    for h in range(2):
                        sp.dma_start(l2_d[bass.ts(p, 1), :, h * HALF:(h + 1) * HALF].rearrange("a q f -> (a q) f"),
                                     lt[64 * h:64 * h + 64, u, :]).then_inc(l2_out[u], 16)

                for p in range(2):
                    load_x(sp, p, x_in2[p])
                    load_l1(p, p)
                sp.wait_ge(x_in2[0], NX)
                load_x(sp, 2, x_in2[0])
                x3_and_signs(0, 0)
                with sp.Fori(0, pairs // 2 - 2) as i:
                    for u in range(2):
                        step(2 * i + u, u, False)
                        load_l1(2 * i + u + 2, u)
                        settle(sp)
                        sp.wait_ge(x3_out[u], NX * i + NX)
                        load_x(sp, 2 * i + u + 3, x_in2[1 - u])
                step(pairs - 4, 0, False)
                load_l1(pairs - 2, 0)
                sp.wait_ge(x3_out[0], NX * (pairs // 2 - 1))
                load_x(sp, pairs - 1, x_in2[1])
                step(pairs - 3, 1, False)
                load_l1(pairs - 1, 1)
                step(pairs - 2, 0, False)
                step(pairs - 1, 1, True)
                for u in range(2):
                    sp.wait_ge(x3_out[u], NX * (pairs // 2))
                    sp.wait_ge(l2_out[u], NL * (pairs // 2))

            @block.vector
            def _(dve):
                def x3a(p, i, u):
                    wait(dve, sign2_ok, p - 1)
                    dve.tensor_copy(af[:, u, :], aff[:, bass.ts(p, 1), :].rearrange("p a k -> p (a k)")).then_inc(af_ok, 1)
                    dve.wait_ge(af_ok, p + 1)
                    dve.wait_ge(ta_ok, p + 1)
                    dve.scalar_tensor_tensor(out=x_of(p, 0), in0=x_of(p, 0), scalar=af[:, u, 0:1],
                                             in1=lin[:, u, :], op0=ALU.mult, op1=ALU.add).then_inc(x3a_ok, 1)

                def leaky(p, i, u):
                    dve.wait_ge(evac2_ok, NCH * (p + 1))
                    dve.scalar_tensor_tensor(out=lt[:, u, :], in0=lt[:, u, :], scalar=SLOPE, in1=lt[:, u, :],
                                             op0=ALU.mult, op1=ALU.max).then_inc(leaky2_ok, 1)
                    dve.wait_ge(leaky2_ok, p + 1)
                    for c in range(NCH):
                        b = dve.bn_stats(st_l[:, bass.ts(p, 1), c, :].rearrange("p a f -> p (a f)"),
                                         lt[:, u, CN * c:CN * (c + 1)])
                    b.then_inc(stat2_ok, 1)
                    dve.wait_ge(stat2_ok, p + 1)

                def step(p, i, u, last):
                    if not last:
                        x3a(p + 1, i + u, 1 - u)
                    leaky(p, i, u)

                x3a(0, 0, 0)
                with dve.Fori(0, pairs // 2 - 1) as i:
                    for u in range(2):
                        step(2 * i + u, i, u, False)
                step(pairs - 2, pairs // 2 - 1, 0, False)
                step(pairs - 1, pairs // 2 - 1, 1, True)

            @block.scalar
            def _(act):
                def x3_and_signs(p, i, u):
                    act.wait_ge(l1_in[u], 16 * i + 16)
                    act.wait_ge(af_ok, p + 1)
                    act.activation(lin[:, u, :], lin[:, u, :], ACT.Identity, scale=sc[:, ALPHA:ALPHA + 1],
                                   bias=af[:, u, 1:2]).then_inc(ta_ok, 1)
                    settle(act)
                    act.wait_ge(x_in2[u], NX * i + NX)
                    act.activation(x_of(p, 1), x_of(p, 1), ACT.Identity, scale=af[:, u, 2:3],
                                   bias=af[:, u, 3:4]).then_inc(x3b_ok, 1)
                    settle(act)
                    act.wait_ge(x3b_ok, p + 1)
                    wait(act, signs2[u], NS * i)
                    act.activation(sg[:, u, 1, :, 1:1 + W], rows(x_of(p, 1)), ACT.Sign)
                    settle(act)
                    act.wait_ge(x3a_ok, p + 1)
                    act.activation(sg[:, u, 0, :, 1:1 + W], rows(x_of(p, 0)),
                                   ACT.Sign).then_inc(sign2_ok, 1)

                def step(p, i, u, last):
                    wait(act, l2_out[u], NL * i)
                    for c in range(NCH):
                        if c == 1 and not last:
                            x3_and_signs(p + 1, i + u, 1 - u)
                        evacuate(act, u, c, conv2_ok, NCH * p + c + 1, evac2_ok)

                x3_and_signs(0, 0, 0)
                with act.Fori(0, pairs // 2 - 1) as i:
                    for u in range(2):
                        step(2 * i + u, i, u, False)
                step(pairs - 2, pairs // 2 - 1, 0, False)
                step(pairs - 1, pairs // 2 - 1, 1, True)

            @block.tensor
            def _(pe):
                def step(p, i, u):
                    pe.wait_ge(signs2[u], NS * i + NS)
                    for c in range(NCH):
                        wait(pe, evac2_ok, NCH * (p - 1) + c + 1)
                        conv_chunk(pe, 1, u, c, conv2_ok)

                step(0, 0, 0)
                step(1, 0, 1)
                with pe.Fori(1, pairs // 2) as i:
                    for u in range(2):
                        step(2 * i + u, i, u)

        fold3, avg3_ok, var3_ok, eps3_ok, rstd3_ok = map(sem, ("fold3", "avg3_ok", "var3_ok", "eps3_ok", "rstd3_ok"))
        M3, E3, V3, R3, A3, K3 = range(6)
        with nc.Block() as block:
            @block.vector
            def _(dve):
                then = steps(dve, fold3)
                c = lambda n: sc[:, n:n + 1]
                then(dve.bn_aggr(mv[:, 0, :], st_l[:, :, :, :].rearrange("p a c f -> p (a c f)")))
                then(dve.tensor_copy(c(M3), mv[:, 0, 0:1]))
                then(dve.tensor_tensor(c(E3), c(M3), c(M3), ALU.mult))
                then(dve.tensor_tensor(c(E3), c(E3), mv[:, 0, 1:2], ALU.add))
                dve.wait_ge(avg3_ok, 1)
                then(dve.tensor_copy(sc[:, M3:E3 + 1], ps[:, 0:2]))
                then(dve.tensor_tensor(c(V3), c(M3), c(M3), ALU.mult))
                dve.tensor_tensor(c(V3), c(E3), c(V3), ALU.subtract).then_inc(var3_ok, 1)
                dve.wait_ge(rstd3_ok, 1)
                then(dve.tensor_tensor(c(A3), prm[:, G3:G3 + 1], c(R3), ALU.mult))
                then(dve.tensor_tensor(c(K3), c(A3), c(M3), ALU.mult))
                then(dve.tensor_tensor(c(K3), prm[:, B3:B3 + 1], c(K3), ALU.subtract))
                dve.wait_ge(avg3_ok, 2)
                then(dve.tensor_copy(ab3[:, :], ps[:, 0:2]))

            @block.tensor
            def _(pe):
                pe.wait_ge(fold3, 4)
                pe.matmul(ps[:, 0:2], avg[:, 1, :], sc[:, M3:E3 + 1], start=True, stop=True).then_inc(avg3_ok, 1)
                pe.wait_ge(fold3, 9)
                pe.matmul(ps[:, 0:2], avg[:, 2, :], sc[:, A3:K3 + 1], start=True, stop=True).then_inc(avg3_ok, 1)

            @block.gpsimd
            def _(pool):
                pool.wait_ge(var3_ok, 1)
                pool.tensor_scalar(sc[:, R3:R3 + 1], sc[:, V3:V3 + 1], EPS, None, ALU.add).then_inc(eps3_ok, 1)
                pool.wait_ge(eps3_ok, 1)
                pool.tensor_tensor(sc[:, R3:R3 + 1], sc[:, R3:R3 + 1], half[:, 0:1], ALU.pow).then_inc(rstd3_ok, 1)


def l1_pass(nc, x, x3_d, l2_d, ab3, flag, con3, wts3, omb, vpb, out, pairs):
    ctx = ExitStack()
    with ctx:
        def sb(name, shape, dt=f32):
            return ctx.enter_context(nc.sbuf_tensor(name, shape, dt))

        def sem(name):
            return ctx.enter_context(nc.semaphore(name))

        def pm(name, cols):
            return ctx.enter_context(nc.psum_tensor(name, [128, cols], f32))

        cst = sb("cst", [128, 2, 128])
        wts = sb("wts", [128, W3])
        ombt = sb("ombt", [LANES, OMC])
        vb = sb("vb", [LANES, 3, C])
        y = sb("y", [128, 2, HW])
        x3h = sb("x3h", [128, PIECE])
        l2h = sb("l2h", [128, PIECE])
        xp = sb("xp", [128, HH + 4, 2, PW])
        omin = sb("omin", [128, HH, 2, PW])
        dwt = sb("dwt", [128, TAPS, DR * LANES // PW * W])
        v5 = sb("v5", [LANES, S, WIN, HH + 4, C])
        oms = sb("oms", [LANES, 2, RP, 3 * GK2])
        ht = sb("ht", [LANES, 3, RP, 2 * GK2])
        hj = sb("hj", [LANES, RP, 2 * GK2])
        mh = sb("mh", [LANES, 3, RP, GK2])
        pr = sb("pr", [LANES, 3, 3, RP, GK2])
        prod = sb("prod", [LANES, SLOTS, RP, WIN, 2 * C])
        accs = sb("accs", [LANES, BR, C])
        tsb = sb("tsb", [128, BR // 2, LANES])
        bn3 = sb("bn3", [128, HW // BN3, BN_F])
        mv3 = sb("mv3", [128, 2])
        rh3 = sb("rh3", [128, 2])
        g3 = sb("g3", [128, 4])
        eps = sb("eps3", [128, 2])
        spare = sb("spare3", [128, 1])
        minus1 = sb("minus1", [LANES, 1])
        far = sb("far", [LANES, S * NBLK * pairs])
        om_p = pm("om_p", 2 * BANK)
        win_p = [pm("win_p0", 2 * BANK), pm("win_p1", 2 * BANK)]
        acc_p = pm("acc_p", BANK)
        misc = pm("misc", BANK)
        ident = cst[0:LANES, 1, 0:LANES]
        omw = wts[:, 0:OMC]
        vpw = wts[:, OMC:OMC + C]
        opw = wts[:, OMC + C:OMC + 3 * C].rearrange("p (y c) -> p y c", y=2)
        dww = wts[:, OMC + 3 * C:OMC + 3 * C + TAPS]
        dwb = wts[:, OMC + 3 * C + TAPS:W3]

        con_in, vb_zero, zeroed, cleared3 = map(sem, ("con3_in", "vb_zero", "zeroed", "cleared3"))
        with nc.Block() as block:
            @block.sync
            def _(sp):
                sp.dma_start(cst[:, :, :], con3).then_inc(con_in, 16)
                sp.dma_start(wts[:, :], wts3).then_inc(con_in, 16)
                sp.dma_start(ombt[:, :], omb).then_inc(con_in, 16)
                sp.wait_ge(vb_zero, 1)
                for h in range(2):
                    for k in (1, 2 * (1 - h)):
                        sp.dma_start(vb[PW * h + 1:PW * h + 1 + W, k, :], vpb[0:W, :]).then_inc(con_in, 16)
                sp.wait_ge(con_in, 7 * 16)

            @block.vector
            def _(dve):
                dve.memset(vb[:, :, :], 0.0).then_inc(vb_zero, 1)
                dve.memset(xp[:, :, :, :], 0.0).then_inc(zeroed, 1)
                dve.wait_ge(zeroed, 1)

            @block.gpsimd
            def _(pool):
                pool.memset(omin[:, :, :, :], 0.0)
                pool.memset(l2h[:, :], 0.0)
                pool.memset(eps[:, 0:1], EPS)
                pool.memset(eps[:, 1:2], -0.5)
                pool.memset(minus1[:, :], -1.0)
                pool.memset(far[:, :], 0.0).then_inc(cleared3, 1)
                pool.wait_ge(cleared3, 1)

        y_in = [sem("y_in0"), sem("y_in1")]
        xl_in, b3_ok, y_ok, bn3_ok, mv3_ok, sq3_ok, rh3_ok, gr3_ok, neg3_ok, sq4_ok, vr3_ok, ep3_ok, rs3_ok, nb3_ok, xp_ok = map(sem, (
            "xl_in", "b3_ok", "y_ok", "bn3_ok", "mv3_ok", "sq3_ok", "rh3_ok", "gr3_ok", "neg3_ok", "sq4_ok", "vr3_ok",
            "ep3_ok", "rs3_ok", "nb3_ok", "xp_ok"))
        v_clear, v_ready, v_ok = sem("v_clear"), sem("v_ready"), sem("v_ok")
        v_in = [sem("v_in0"), sem("v_in1")]
        tap_ok, dw1_ok, dw2_ok, dw3_ok, dw_ok = map(sem, ("tap_ok", "dw1_ok", "dw2_ok", "dw3_ok", "dw_ok"))
        om_ready, om_ok, abs_ok, hat_ok, mh_ok, pr_ok = map(sem, ("om_ready", "om_ok", "abs_ok", "hat_ok", "mh_ok", "pr_ok"))
        win_ok, prod_ok, fold_ok, pre_ok, add_ok, accs_ok, t_ready, t_ok, o_ready, o_ok, out_ok = map(sem, (
            "win_ok", "prod_ok", "fold_ok", "pre_ok", "add_ok", "accs_ok", "t_ready", "t_ok", "o_ready", "o_ok", "out_ok"))

        NB2 = S * NBLK
        NV = 4 * 16
        KV = (HH + 4) // VR

        DW_AT = (0, 1, 2, 3, 5, 6, 7, 9, 10, 11, 13, 14)
        FIRST = 6
        FOLD_COLS = (5, 0, 0)
        DIRECT = (2, 4)

        def last_user(n):
            n = n - SLOTS
            return n if n >= 0 else max(m for m in range(-SLOTS, 0) if (m + WIN * NB2) % SLOTS == n % SLOTS)

        def chunks(j):
            if j >= NBLK:
                return [(1, c) for c in range(DW_AT[j - NBLK], DW_AT[j - NBLK + 1])]
            if j + NBLK + 1 < len(DW_AT):
                return [(0, c) for c in range(DW_AT[j + NBLK], DW_AT[j + NBLK + 1])]
            return []

        def chunks_now(i, j, first, last):
            if first and j < NBLK:
                return [(i, c) for c in range(FIRST + 2 * j, min(FIRST + 2 * j + 2, NB2))]
            return [(i + ahead, c) for ahead, c in chunks(j) if not (last and ahead)]

        def folds(j, d):
            return d < FOLD_COLS[len(chunks(j))]

        def adds(j, d):
            return not (len(chunks(j)) == 2 and d in DIRECT)

        def columns(what, j, d):
            return sum(what(k, e) for k in range(NB2) for e in range(WIN) if (k, e) < (j, d))

        def where(j):
            return j // NBLK, j % NBLK

        with nc.Block() as block:
            @block.sync
            def _(sp):
                def load_pair(q):
                    for s in range(S):
                        sp.dma_start(y[64 * s:64 * s + 64, bass.ts(q % 2, 1), :].rearrange("p a f -> p (a f)"),
                                     x[S * q + s, :, :]).then_inc(y_in[s], 16)

                def load_piece(q, k):
                    wait(sp, y_ok, PIECES * q + k)
                    at = slice(PIECE * k, PIECE * (k + 1))
                    for s in range(S):
                        sp.dma_start(x3h[64 * s:64 * s + 64, :], x3_d[S * q + s, :, at]).then_inc(xl_in, 16)
                        sp.dma_start(l2h[64 * s:64 * s + CO, :],
                                     l2_d[bass.ts(q, 1), CO * s:CO * (s + 1), at].rearrange("a c f -> (a c) f")).then_inc(xl_in, 16)

                def shift_values(q, s):
                    sp.wait_ge(v_ok, KV * (S * q + s + 1))
                    for d in (0, 1, 3, 4):
                        to, fr = max(0, 2 - d), max(0, d - 2)
                        n = LANES - abs(d - 2)
                        sp.dma_start(v5[to:to + n, s, d, :, :], v5[fr:fr + n, s, 2, :, :]).then_inc(v_in[s], 16)

                def store(q, s):
                    sp.wait_ge(o_ok, NB2 * q + NBLK * (s + 1))
                    sp.dma_start(out[S * q + s, :, :],
                                 y[64 * s:64 * s + 64, bass.ts(q % 2, 1), :].rearrange("p a f -> p (a f)")).then_inc(out_ok, 16)

                def pair(i, first, last):
                    if not first:
                        store(i - 1, 1)
                    if not last:
                        wait(sp, out_ok, 16 * S * i)
                        load_pair(i + 1)
                        for k in range(PIECES):
                            load_piece(i + 1, k)
                    shift_values(i, 1)
                    store(i, 0)
                    if not last:
                        shift_values(i + 1, 0)

                load_pair(0)
                for k in range(PIECES):
                    load_piece(0, k)
                sp.wait_ge(v_clear, 1)
                shift_values(0, 0)
                pair(0, True, False)
                with sp.Fori(1, pairs - 1) as i:
                    pair(i, False, False)
                pair(pairs - 1, False, True)
                store(pairs - 1, 1)
                sp.wait_ge(out_ok, 16 * S * pairs)

            @block.vector
            def _(dve):
                def sum_piece(q, h):
                    at = slice(PIECE * h, PIECE * (h + 1))
                    yh = y[:, bass.ts(q % 2, 1), at].rearrange("p a f -> p (a f)")
                    if h == 0:
                        for s in range(S):
                            dve.wait_ge(y_in[s], 16 * q + 16)
                    dve.wait_ge(xl_in, 64 * (PIECES * q + h + 1))
                    dve.scalar_tensor_tensor(out=yh, in0=yh, scalar=ab3[:, 1:2], in1=x3h[:, :],
                                             op0=ALU.add, op1=ALU.add).then_inc(b3_ok, 1)
                    dve.wait_ge(b3_ok, PIECES * q + h + 1)
                    dve.scalar_tensor_tensor(out=yh, in0=l2h[:, :], scalar=ab3[:, 0:1], in1=yh,
                                             op0=ALU.mult, op1=ALU.add).then_inc(y_ok, 1)

                def channel_stats(q):
                    dve.wait_ge(y_ok, PIECES * q + PIECES)
                    dve.tensor_copy(spare[:, :], cst[:, 0, 0:1])
                    for c in range(HW // BN3):
                        b = dve.bn_stats(bn3[:, c, :], y[:, bass.ts(q % 2, 1), BN3 * c:BN3 * (c + 1)].rearrange("p a f -> p (a f)"))
                    b.then_inc(bn3_ok, 1)
                    dve.wait_ge(bn3_ok, q + 1)
                    dve.tensor_copy(spare[:, :], bn3[:, 0, 0:1])
                    dve.bn_aggr(mv3[:, :], bn3[:, :, :].rearrange("p c f -> p (c f)")).then_inc(mv3_ok, 1)
                    dve.wait_ge(mv3_ok, q + 1)
                    dve.tensor_copy(rh3[:, 0:1], mv3[:, 0:1])
                    dve.tensor_tensor(rh3[:, 1:2], mv3[:, 0:1], mv3[:, 0:1], ALU.mult).then_inc(sq3_ok, 1)
                    dve.wait_ge(sq3_ok, q + 1)
                    dve.tensor_tensor(rh3[:, 1:2], rh3[:, 1:2], mv3[:, 1:2], ALU.add).then_inc(rh3_ok, 1)

                def group_stats(q):
                    dve.wait_ge(gr3_ok, q + 1)
                    dve.tensor_scalar(g3[:, 0:1], misc[:, 0:1], -1.0, None, ALU.mult).then_inc(neg3_ok, 1)
                    dve.wait_ge(neg3_ok, q + 1)
                    dve.tensor_tensor(g3[:, 1:2], misc[:, 0:1], g3[:, 0:1], ALU.mult).then_inc(sq4_ok, 1)
                    dve.wait_ge(sq4_ok, q + 1)
                    dve.tensor_tensor(g3[:, 1:2], g3[:, 1:2], misc[:, 1:2], ALU.add).then_inc(vr3_ok, 1)

                def bias_values(q, s, v):
                    dve.wait_ge(v_ready, KV * (S * q + s) + v + 1)
                    edge = {0: ((0, 2, 0), (2, VR, 1)), KV - 1: ((0, VR - 2, 1), (VR - 2, VR, 2))}
                    parts = edge.get(v, ((0, VR, 1),))
                    for a, z, k in parts:
                        ins = dve.tensor_tensor(
                            v5[:, s, 2, VR * v + a:VR * v + z, :],
                            misc[0:LANES, C * a:C * z].rearrange("p (r c) -> p r c", c=C),
                            vb[:, k:k + 1, :].broadcast_to([LANES, z - a, C]), ALU.add)
                    ins.then_inc(v_ok, 1)

                def copy_om(t, j):
                    dve.wait_ge(om_ready, t + 1)
                    for p in range(RP):
                        ins = dve.tensor_tensor(
                            oms[:, j % 2, p, :].rearrange("q (k r g) -> q r k g", r=2, g=G),
                            om_p[0:LANES, BANK * p:BANK * (p + 1)].rearrange("q (r k) -> q r k", r=2)[:, :, 0:OMC],
                            ombt[:, :].unsqueeze(1).broadcast_to([LANES, 2, OMC]), ALU.add)
                    ins.then_inc(om_ok, 1)

                def mask_hats(t, j):
                    dve.wait_ge(hat_ok, t + 1)
                    dve.tensor_tensor(mh[:, :, :, :],
                                      oms[:, j % 2, :, 2 * GK2:3 * GK2].unsqueeze(1).broadcast_to([LANES, 3, RP, GK2]),
                                      ht[:, :, :, 0:GK2], ALU.mult).then_inc(mh_ok, 1)

                def products(t, a):
                    if a == 0:
                        wait(dve, win_ok, t)
                        dve.wait_ge(mh_ok, t + 1)
                    dve.tensor_tensor(pr[:, a, :, :, :],
                                      mh[:, a:a + 1, :, :].broadcast_to([LANES, 3, RP, GK2]),
                                      ht[:, :, :, GK2:2 * GK2], ALU.mult).then_inc(pr_ok, 1)

                def multiply(i, t, j, d):
                    s, b = where(j)
                    if d == 0:
                        dve.wait_ge(win_ok, t + 1)
                        if b == 0:
                            dve.wait_ge(v_in[s], NV * (i + 1))
                    slot = (WIN * j + d) % SLOTS
                    wait(dve, add_ok, WIN * (t - j) + last_user(WIN * j + d) + 1)
                    cells = WIN * 2 * G
                    wgt = win_p[j % 2][0:LANES, :].rearrange("q (p z) -> q p z", p=RP)[:, :, cells * d:cells * (d + 1)]
                    row = v5[:, s, d, BR * b:BR * b + BR, :]
                    val = bass.AP(row.tensor, row.offset, [row.ap[0], [2 * C, RP], [C, WIN], [1, 2 * C]])
                    dve.tensor_tensor(prod[:, slot, :, :, :].rearrange("q p a (z c) -> q p (a z) c", c=C // G),
                                      wgt.unsqueeze(3).broadcast_to([LANES, RP, cells, C // G]), val, ALU.mult).then_inc(prod_ok, 1)

                def add_output(i, t, j):
                    s, b = where(j)
                    dve.wait_ge(o_ready, t + 1)
                    rows4 = y[64 * s:64 * s + 64, bass.ts(i % 2, 1), :].rearrange(
                        "p a (h z r e w) -> p h e r (a z) w", h=2, r=RP, e=2, w=W)[:, :, :, :, b, :]
                    moved = misc[64 * s:64 * s + 64, 0:BR * LANES].rearrange(
                        "p (e r h w) -> p h e r w", e=2, r=RP, h=2)[:, :, :, :, 1:1 + W]
                    for h in range(2):
                        ins = dve.tensor_tensor(rows4[:, h], rows4[:, h], moved[:, h], ALU.add)
                    ins.then_inc(o_ok, 1)

                def step(i, j, first, last):
                    t = NB2 * i + j
                    more = lambda n: not last or j + n < NB2
                    multiply(i, t, j, 0)
                    if more(1):
                        mask_hats(t + 1, j + 1)
                        products(t + 1, 0)
                    if 2 <= j <= KV + 1:
                        bias_values(i, 1, j - 2)
                    if not last and NBLK + 2 <= j <= NBLK + KV + 1:
                        bias_values(i + 1, 0, j - NBLK - 2)
                    multiply(i, t, j, 1)
                    if more(1):
                        products(t + 1, 1)
                    multiply(i, t, j, 2)
                    if more(2):
                        copy_om(t + 2, j + 2)
                    if more(1):
                        products(t + 1, 2)
                    multiply(i, t, j, 3)
                    if j > 0:
                        add_output(i, t - 1, j - 1)
                    elif not first:
                        add_output(i - 1, t - 1, NB2 - 1)
                    multiply(i, t, j, 4)
                    if not last:
                        if 1 <= j <= PIECES:
                            sum_piece(i + 1, j - 1)
                        if j == PIECES:
                            channel_stats(i + 1)
                        if j == 5:
                            group_stats(i + 1)

                for k in range(PIECES):
                    sum_piece(0, k)
                channel_stats(0)
                group_stats(0)
                for v in range(KV):
                    bias_values(0, 0, v)
                copy_om(0, 0)
                copy_om(1, 1)
                mask_hats(0, 0)
                for a in range(3):
                    products(0, a)
                for j in range(NB2):
                    step(0, j, True, False)
                with dve.Fori(1, pairs - 1) as i:
                    for j in range(NB2):
                        step(i, j, False, False)
                for j in range(NB2):
                    step(pairs - 1, j, False, True)
                add_output(pairs - 1, NB2 * pairs - 1, NB2 - 1)

            @block.gpsimd
            def _(pool):
                def deviation(q):
                    pool.wait_ge(vr3_ok, q + 1)
                    wait(pool, xp_ok, q)
                    pool.tensor_tensor(g3[:, 2:3], g3[:, 1:2], eps[:, 0:1], ALU.add).then_inc(ep3_ok, 1)
                    pool.wait_ge(ep3_ok, q + 1)
                    pool.tensor_tensor(g3[:, 2:3], g3[:, 2:3], eps[:, 1:2], ALU.pow).then_inc(rs3_ok, 1)
                    pool.wait_ge(rs3_ok, q + 1)
                    pool.tensor_tensor(g3[:, 3:4], g3[:, 0:1], g3[:, 2:3], ALU.mult).then_inc(nb3_ok, 1)

                def depthwise(q, c, part):
                    n = NB2 * q + c
                    b, h = c // 2, c % 2
                    if part == 0:
                        pool.wait_ge(tap_ok, n + 1)
                        pool.tensor_tensor(dwt[:, 0:4, :], dwt[:, 0:4, :], dwt[:, 4:8, :], ALU.add).then_inc(dw1_ok, 1)
                        return
                    pool.wait_ge(dw1_ok, n + 1)
                    pool.tensor_tensor(dwt[:, 0:2, :], dwt[:, 0:2, :], dwt[:, 2:4, :], ALU.add).then_inc(dw2_ok, 1)
                    pool.wait_ge(dw2_ok, n + 1)
                    pool.tensor_tensor(dwt[:, 0, :], dwt[:, 0, :], dwt[:, 1, :], ALU.add).then_inc(dw3_ok, 1)
                    wait(pool, om_ready, NB2 * (q - 1) + NBLK + b + 1)
                    pool.wait_ge(dw3_ok, n + 1)
                    r = BR * b + DR * h
                    pool.tensor_tensor(omin[:, r:r + DR, :, 1:1 + W], dwt[:, 0, :].rearrange("p (r h w) -> p r h w", h=2, w=W),
                                       dwt[:, 8, :].rearrange("p (r h w) -> p r h w", h=2, w=W), ALU.add).then_inc(dw_ok, 1)

                def add_rows(i, t, j, d):
                    slot = (WIN * j + d) % SLOTS
                    pool.wait_ge(prod_ok, WIN * t + d + 1)
                    ins = pool.tensor_tensor(prod[:, slot, :, 0:2, :], prod[:, slot, :, 0:2, :], prod[:, slot, :, 2:4, :], ALU.add)
                    if folds(j, d):
                        ins.then_inc(fold_ok, 1)
                        pool.wait_ge(fold_ok, columns(folds, NB2, 0) * i + columns(folds, j, d) + 1)
                        ins = pool.tensor_tensor(prod[:, slot, :, 0, :], prod[:, slot, :, 0, :], prod[:, slot, :, 1, :], ALU.add)
                    ins.then_inc(pre_ok, 1)

                def step(i, j, first, last):
                    todo = chunks_now(i, j, first, last)
                    for d in range(WIN):
                        if adds(j, d):
                            add_rows(i, NB2 * i + j, j, d)
                        if 1 <= d <= 2 * len(todo):
                            depthwise(*todo[(d - 1) // 2], (d - 1) % 2)
                    if not last and j == NBLK - 2:
                        deviation(i + 1)

                for s in range(S):
                    pool.memset(v5[:, s, 0:2, :, :], 0.0)
                    clear = pool.memset(v5[:, s, 3:5, :, :], 0.0)
                clear.then_inc(v_clear, 1)
                deviation(0)
                for c in range(FIRST):
                    depthwise(0, c, 0)
                    depthwise(0, c, 1)
                for j in range(NB2):
                    step(0, j, True, False)
                with pool.Fori(1, pairs - 1) as i:
                    for j in range(NB2):
                        step(i, j, False, False)
                for j in range(NB2):
                    step(pairs - 1, j, False, True)

            @block.scalar
            def _(act):
                def normalise(q):
                    act.wait_ge(nb3_ok, q + 1)
                    wait(act, v_ready, KV * S * q)
                    for h, r in ((0, 2), (1, 0)):
                        at = HH * h + r - 2
                        ins = act.activation(xp[:, r:r + HH + 2, h, 1:1 + W],
                                             y[:, bass.ts(q % 2, 1), W * at:W * (at + HH + 2)].rearrange("p a (r w) -> p (a r) w", w=W),
                                             ACT.Identity, scale=g3[:, 2:3], bias=g3[:, 3:4])
                    ins.then_inc(xp_ok, 1)

                def taps(q, c):
                    n = NB2 * q + c
                    b, h = c // 2, c % 2
                    wait(act, dw_ok, n)
                    act.wait_ge(xp_ok, q + 1)
                    r = BR * b + DR * h + 1
                    for k in range(TAPS):
                        ins = act.activation(dwt[:, k, :].rearrange("p (r h w) -> p r h w", h=2, w=W),
                                             xp[:, r + k // 3:r + k // 3 + DR, :, k % 3:k % 3 + W],
                                             ACT.Identity, scale=dww[:, k:k + 1], bias=dwb if k == TAPS - 1 else 0.0)
                    ins.then_inc(tap_ok, 1)

                def hats(t, j):
                    u = j % 2
                    off = oms[:, u, :, 0:2 * GK2]
                    wait(act, pr_ok, 3 * t)
                    act.wait_ge(om_ok, t + 1)
                    act.activation(ht[:, 1, :, :], off, ACT.Abs).then_inc(abs_ok, 1)
                    act.activation(ht[:, 0, :, :], off, ACT.Relu, scale=-1.0)
                    act.activation(ht[:, 2, :, :], off, ACT.Relu)
                    act.wait_ge(abs_ok, t + 1)
                    act.activation(hj[:, :, :], ht[:, 1, :, :], ACT.Relu, bias=minus1[:, :], accum_out=far[:, bass.ts(t, 1)])
                    act.activation(ht[:, 1, :, :], ht[:, 1, :, :], ACT.Identity, scale=-1.0, bias=1.0).then_inc(hat_ok, 1)

                def copy_acc(t):
                    act.wait_ge(add_ok, WIN * (t + 1))
                    act.activation(accs[:, :, :], acc_p[0:LANES, 0:BR * C].rearrange("p (r c) -> p r c", c=C),
                                   ACT.Copy).then_inc(accs_ok, 1)

                def copy_t(t):
                    act.wait_ge(t_ready, t + 1)
                    act.activation(tsb[:, :, :], misc[:, 0:BR // 2 * LANES].rearrange("p (r l) -> p r l", l=LANES),
                                   ACT.Copy).then_inc(t_ok, 1)

                def step(i, j, first, last):
                    t = NB2 * i + j
                    before = j > 0 or not first
                    if before:
                        copy_acc(t - 1)
                    todo = chunks_now(i, j, first, last)
                    if todo:
                        taps(*todo[0])
                    if before:
                        copy_t(t - 1)
                    if not last and j == NBLK - 1:
                        normalise(i + 1)
                    if not last or j + 2 < NB2:
                        hats(t + 2, j + 2)
                    if todo[1:]:
                        taps(*todo[1])

                normalise(0)
                for c in range(FIRST):
                    taps(0, c)
                hats(0, 0)
                hats(1, 1)
                for j in range(NB2):
                    step(0, j, True, False)
                with act.Fori(1, pairs - 1) as i:
                    for j in range(NB2):
                        step(i, j, False, False)
                for j in range(NB2):
                    step(pairs - 1, j, False, True)
                copy_acc(NB2 * pairs - 1)
                copy_t(NB2 * pairs - 1)

            @block.tensor
            def _(pe):
                def groups(q):
                    pe.wait_ge(rh3_ok, q + 1)
                    pe.matmul(misc[:, 0:2], cst[:, 0, :], rh3[:, :], start=True, stop=True).then_inc(gr3_ok, 1)

                def values(q, s, v):
                    pe.wait_ge(xp_ok, q + 1)
                    for k in range(VR):
                        r = VR * v + k
                        mm = pe.matmul(misc[0:LANES, C * k:C * (k + 1)],
                                       xp[64 * s:64 * s + 64, r, :, :].rearrange("p h w -> p (h w)"),
                                       vpw[64 * s:64 * s + 64, :], start=True, stop=True)
                    mm.then_inc(v_ready, 1)

                def offsets(q, t, j):
                    s, b = where(j)
                    pe.wait_ge(dw_ok, NB2 * q + 2 * (b + 1))
                    wait(pe, om_ok, t)
                    for r in range(BR):
                        rows2 = omin[64 * s:64 * s + 64, BR * b + r, :, :].rearrange("p h w -> p (h w)")
                        mm = pe.matmul(om_p[0:LANES, 256 * r:256 * r + OMC], rows2, omw[64 * s:64 * s + 64, :],
                                       start=True, stop=True)
                    mm.then_inc(om_ready, 1)

                def windows(t, j, a):
                    pe.wait_ge(pr_ok, 3 * t + a + 1)
                    if a == 0:
                        wait(pe, prod_ok, WIN * (t - 1))
                    for p in range(RP):
                        at = win_p[j % 2][0:LANES, BANK * p:BANK * p + WIN * WIN * 2 * G]
                        at = at.rearrange("q (e a z) -> q a e z", e=WIN, a=WIN)
                        for e in range(3):
                            mm = pe.matmul(at[:, a:a + 3, e:e + 3, :], ident, pr[:, a, e, p, :],
                                           start=(a == 0 and e == 0), stop=(a == 2 and e == 2), skip_group_check=True)
                    if a == 2:
                        mm.then_inc(win_ok, 1)

                def sums(i, j, d):
                    t = NB2 * i + j
                    if d == 0:
                        wait(pe, accs_ok, t)
                    if adds(j, d):
                        pe.wait_ge(pre_ok, columns(adds, NB2, 0) * i + columns(adds, j, d) + 1)
                    else:
                        pe.wait_ge(prod_ok, WIN * t + d + 1)
                    slot = (WIN * j + d) % SLOTS
                    left = (0, 4) if folds(j, d) else (0, 1, 4) if adds(j, d) else range(WIN)
                    for a in left:
                        mm = pe.matmul(acc_p[0:LANES, 0:BR * C], ident, prod[:, slot, :, a, :],
                                       start=(d == 0 and a == 0), stop=(d == WIN - 1 and a == 4))
                    mm.then_inc(add_ok, 1)

                def turn(t, j):
                    pe.wait_ge(accs_ok, t + 1)
                    for r in range(BR // 2):
                        mm = pe.matmul(misc[:, LANES * r:LANES * (r + 1)], accs[:, 2 * r:2 * r + 2, :], ident,
                                       start=True, stop=True)
                    mm.then_inc(t_ready, 1)

                def project(t, j):
                    s, b = where(j)
                    pe.wait_ge(t_ok, t + 1)
                    for e in range(2):
                        mm = pe.matmul(misc[64 * s:64 * s + 64, 2 * LANES * e:2 * LANES * (e + 1)], opw[:, e, :], tsb[:, :, :],
                                       start=True, stop=True)
                    mm.then_inc(o_ready, 1)

                def step(i, j, first, last):
                    t = NB2 * i + j
                    before = j > 0 or not first
                    after = not last or j + 1 < NB2
                    if not last or j + 2 < NB2:
                        if j + 2 < NB2:
                            offsets(i, t + 2, j + 2)
                        else:
                            offsets(i + 1, t + 2, j + 2 - NB2)
                    sums(i, j, 0)
                    if before:
                        if 1 <= j - 1 <= KV:
                            pe.wait_ge(v_ok, KV * S * i + KV + j - 1)
                        if not last and NBLK + 1 <= j - 1 <= NBLK + KV:
                            pe.wait_ge(v_ok, KV * S * (i + 1) + j - 1 - NBLK)
                        if not last and j == NBLK - 1:
                            pe.wait_ge(vr3_ok, i + 2)
                        wait(pe, o_ok, t - 1)
                        turn(t - 1, j - 1)
                    if after:
                        windows(t + 1, j + 1, 0)
                    sums(i, j, 1)
                    if before:
                        project(t - 1, (j - 1) % NB2)
                    if after:
                        windows(t + 1, j + 1, 1)
                    if after:
                        windows(t + 1, j + 1, 2)
                    sums(i, j, 2)
                    sums(i, j, 3)
                    if 1 <= j <= KV:
                        wait(pe, o_ok, t)
                        values(i, 1, j - 1)
                    if not last and NBLK + 1 <= j <= NBLK + KV:
                        wait(pe, o_ok, t)
                        values(i + 1, 0, j - NBLK - 1)
                    if not last and j == NBLK - 2:
                        wait(pe, o_ok, t)
                        groups(i + 1)
                    sums(i, j, 4)

                groups(0)
                pe.wait_ge(vr3_ok, 1)
                for v in range(KV):
                    if v:
                        pe.wait_ge(v_ok, v)
                    values(0, 0, v)
                offsets(0, 0, 0)
                offsets(0, 1, 1)
                for a in range(3):
                    windows(0, 0, a)
                pe.wait_ge(v_ok, KV)
                for j in range(NB2):
                    step(0, j, True, False)
                with pe.Fori(1, pairs - 1) as i:
                    for j in range(NB2):
                        step(i, j, False, False)
                for j in range(NB2):
                    step(pairs - 1, j, False, True)
                pe.wait_ge(o_ok, NB2 * pairs - 1)
                turn(NB2 * pairs - 1, NB2 - 1)
                project(NB2 * pairs - 1, NB2 - 1)

        flag_far(nc, far, flag, misc)


def flag_far(nc, far, flag, total_p):
    with ExitStack() as ctx:
        total = ctx.enter_context(nc.sbuf_tensor("far_total", [LANES, 2], f32))
        summed, joined, flagged = (ctx.enter_context(nc.semaphore(n)) for n in ("far_summed", "far_joined", "far_flagged"))
        with nc.Block() as block:
            @block.vector
            def _(dve):
                dve.memset(total[:, 1:2], 1.0)
                dve.tensor_reduce(total[:, 0:1], far[:, :], AX.X, ALU.add).then_inc(summed, 1)
                dve.wait_ge(joined, 1)
                dve.tensor_scalar(flag[0:1, 0:1], total_p[0:1, 0:1], 0.0, None, ALU.is_gt).then_inc(flagged, 1)
                dve.wait_ge(flagged, 1)

            @block.tensor
            def _(pe):
                pe.wait_ge(summed, 1)
                pe.matmul(total_p[0:1, 0:1], total[:, 0:1], total[:, 1:2], start=True, stop=True).then_inc(joined, 1)


def general_pass(nc, x, x3_d, l2_d, ab3, flag, con3, wts3, omb, vpb, places, vpad, out, samples):
    with ExitStack() as ctx:
        def sb(name, shape, dt=f32):
            return ctx.enter_context(nc.sbuf_tensor(name, shape, dt))

        def sem(name):
            return ctx.enter_context(nc.semaphore(name))

        cst = sb("g_cst", [128, 2, 128])
        wts = sb("g_wts", [128, W3])
        ombt = sb("g_omb", [TP, OMC])
        vbt = sb("g_vpb", [TP, C])
        plc = sb("g_places", [TP, 3, GK])
        zero = sb("g_zero", [VP, VP * C // G])
        y = sb("g_y", [C, HW])
        x3s = sb("g_x3", [C, HW])
        l2s = sb("g_l2", [C, HW])
        xp = sb("g_xp", [C, PW, PW])
        omin = sb("g_omin", [C, HW])
        bn = sb("g_bn", [C, HW // BN3, BN_F])
        mv = sb("g_mv", [C, 2])
        rh = sb("g_rh", [C, 2])
        gst = sb("g_gst", [C, 4])
        eps = sb("g_eps", [C, 2])
        spare = sb("g_spare", [C, 1])
        stage = sb("g_stage", [C, 2, TP])
        vs = sb("g_vs", [TP, C])
        oms = sb("g_oms", [TP, OMC])
        base = sb("g_base", [TP, 2, GK])
        pos = sb("g_pos", [TP, 2, GK])
        low = sb("g_low", [TP, 2, GK])
        over = sb("g_over", [TP, 2, GK])
        whole = sb("g_whole", [TP, 2, GK], i32)
        frac = sb("g_frac", [TP, 2, GK])
        rest = sb("g_rest", [TP, 2, GK])
        mk = sb("g_mk", [TP, 2, GK])
        wt = sb("g_wt", [TP, 4, GK])
        place = sb("g_place", [TP, 4, GK])
        idx = sb("g_idx", [TP, 4, GK], i32)
        got = sb("g_got", [TP, 4, GK, C // G])
        acc = sb("g_acc", [TP, C])
        acct = sb("g_acct", [C, TP])
        ps = [ctx.enter_context(nc.psum_tensor(f"g_ps{k}", [128, BANK], f32)) for k in range(4)]
        st_p, v_p, om_p, o_p = ps
        omw = wts[0:C, 0:OMC]
        vpw = wts[0:C, OMC:OMC + C]
        opw = wts[0:C, OMC + C:OMC + 3 * C]
        dww = wts[0:C, OMC + 3 * C:OMC + 3 * C + TAPS]
        dwb = wts[0:C, OMC + 3 * C + TAPS:W3]

        con_in, zeroed, ready, padded = map(sem, ("g_con_in", "g_zeroed", "g_ready", "g_padded"))
        in_ok, x1_ok, bn_ok, rh_ok, st_ok, var_ok, dev_ok, out_ok = map(sem, (
            "g_in", "g_x1", "g_bn", "g_rh", "g_st", "g_var", "g_dev", "g_out"))
        pool_ok, pre_ok, tile_ok, carrier = map(sem, ("g_pool", "g_pre", "g_tile", "g_carrier"))
        vst_ok, v_ready, vs_ok, v_in = map(sem, ("g_vst", "g_v_ready", "g_vs_ok", "g_v_in"))
        ost_ok, om_ready, idx_ok, got_in, got_ok, acc_ok, t_ready, t_ok, o_ready, y_ok = map(sem, (
            "g_ost", "g_om_ready", "g_idx", "g_got_in", "g_got_ok", "g_acc_ok", "g_t_ready", "g_t_ok", "g_o_ready", "g_y"))

        def chain(eng, done, start):
            n = [0]

            def then(ins):
                n[0] += 1
                ins.then_inc(done, 1)
                eng.wait_ge(done, start + n[0])
            return then, n

        with nc.Block() as block:
            @block.sync
            def _(sp):
                for to, fr in ((cst[:, :, :], con3), (wts[:, :], wts3), (ombt[:, :], omb[0:TP, :]),
                               (vbt[:, :], vpb[0:TP, :])):
                    sp.dma_start(to, fr).then_inc(con_in, 16)
                sp.dma_start(plc[:, :, :], places).then_inc(out_ok, 16)
                sp.wait_ge(zeroed, 1)
                for g in range(G):
                    sp.dma_start(vpad[g * VP * VP:(g + 1) * VP * VP, :].rearrange("(r w) c -> r (w c)", r=VP),
                                 zero[:, :]).then_inc(padded, 16)
                sp.wait_ge(con_in, 4 * 16)
                sp.wait_ge(out_ok, 16)
                sp.wait_ge(padded, G * 16)

            @block.vector
            def _(dve):
                dve.memset(zero[:, :], 0.0).then_inc(zeroed, 1)
                dve.memset(l2s[:, :], 0.0)
                dve.memset(xp[:, :, :], 0.0)
                dve.memset(eps[:, 0:1], EPS)
                dve.memset(eps[:, 1:2], -0.5).then_inc(ready, 1)
                dve.wait_ge(ready, 1)

        PRE = 2 + 4 + 3 + TAPS
        TILE = 15

        with nc.Block() as block:
            @block.sync
            def _(sp):
                far = sp.value_load(flag[0:1, 0:1], min_val=0, max_val=1)
                with sp.If(far > 0):
                    with sp.Fori(0, samples) as n:
                        one = bass.ts(n, 1)
                        sp.wait_ge(con_in, 4 * 16)
                        sp.wait_ge(out_ok, 16 * n + 16)
                        sp.dma_start(y[:, :], x[one, :, :].rearrange("a c f -> (a c) f")).then_inc(in_ok, 16)
                        sp.dma_start(x3s[:, :], x3_d[one, :, :].rearrange("a c f -> (a c) f")).then_inc(in_ok, 16)
                        sp.dma_start(l2s[0:CO, :], l2_d[one, :, :].rearrange("a c f -> (a c) f")).then_inc(in_ok, 16)
                        with sp.Fori(0, TILES) as t:
                            sp.wait_ge(vs_ok, TILES * n + t + 1)
                            for r in range(2):
                                sp.dma_start(
                                    vpad.rearrange("(g r w) c -> r w g c", g=G, r=VP)[bass.ds(2 * t + r + 2, 1), 2:2 + W, :, :].rearrange("a w g c -> (a w) g c"),
                                    vs[W * r:W * (r + 1), :].rearrange("p (g c) -> p g c", g=G)).then_inc(v_in, 16)
                        sp.wait_ge(y_ok, TILES * (n + 1))
                        sp.dma_start(out[one, :, :].rearrange("a c f -> (a c) f"), y[:, :]).then_inc(out_ok, 16)
                    sp.wait_ge(out_ok, 16 * samples + 16)
                sp.wait_ge(con_in, 4 * 16)

            @block.vector
            def _(dve):
                def x1_and_norm(n):
                    then, used = chain(dve, pre_ok, PRE * n)
                    dve.wait_ge(in_ok, 48 * (n + 1))
                    then(dve.scalar_tensor_tensor(out=y[:, :], in0=y[:, :], scalar=ab3[0:C, 1:2], in1=x3s[:, :],
                                                  op0=ALU.add, op1=ALU.add))
                    then(dve.scalar_tensor_tensor(out=y[:, :], in0=l2s[:, :], scalar=ab3[0:C, 0:1], in1=y[:, :],
                                                  op0=ALU.mult, op1=ALU.add))
                    for c in range(HW // BN3):
                        b = dve.bn_stats(bn[:, c, :], y[:, BN3 * c:BN3 * (c + 1)])
                    then(b)
                    dve.tensor_copy(spare[:, :], bn[:, 0, 0:1])
                    then(dve.bn_aggr(mv[:, :], bn[:, :, :].rearrange("p c f -> p (c f)")))
                    dve.tensor_copy(rh[:, 0:1], mv[:, 0:1])
                    then(dve.tensor_tensor(rh[:, 1:2], mv[:, 0:1], mv[:, 0:1], ALU.mult))
                    dve.tensor_tensor(rh[:, 1:2], rh[:, 1:2], mv[:, 1:2], ALU.add).then_inc(rh_ok, 1)
                    dve.wait_ge(st_ok, n + 1)
                    then(dve.tensor_scalar(gst[:, 0:1], st_p[0:C, 0:1], -1.0, None, ALU.mult))
                    then(dve.tensor_tensor(gst[:, 1:2], st_p[0:C, 0:1], gst[:, 0:1], ALU.mult))
                    dve.tensor_tensor(gst[:, 1:2], gst[:, 1:2], st_p[0:C, 1:2], ALU.add).then_inc(var_ok, 1)
                    dve.wait_ge(dev_ok, n + 1)
                    image = y[:, :].rearrange("p (r w) -> p r w", w=W)
                    then(dve.tensor_scalar(xp[:, 1:1 + H, 1:1 + W], image, gst[:, 2:3], gst[:, 3:4], ALU.mult, ALU.add))
                    conv = omin[:, :].rearrange("p (r w) -> p r w", w=W)
                    then(dve.tensor_scalar(conv, xp[:, 0:H, 0:W], dww[:, 0:1], dwb, ALU.mult, ALU.add))
                    for k in range(1, TAPS):
                        then(dve.scalar_tensor_tensor(out=conv, in0=xp[:, k // 3:k // 3 + H, k % 3:k % 3 + W],
                                                      scalar=dww[:, k:k + 1], in1=conv, op0=ALU.mult, op1=ALU.add))
                    then(dve.tensor_copy(base[:, :, :], plc[:, 0:2, :]))
                    dve.tensor_copy(spare[:, :], eps[:, 0:1])
                    assert used[0] == PRE, used

                def values(T, t):
                    dve.tensor_scalar(stage[:, 0, :].rearrange("p (r w) -> p r w", w=W), xp[:, bass.ds(2 * t + 1, 2), 1:1 + W],
                                      1.0, None, ALU.mult).then_inc(vst_ok, 1)
                    dve.wait_ge(v_ready, T + 1)
                    dve.tensor_tensor(vs[:, :], v_p[0:TP, 0:C], vbt[:, :], ALU.add).then_inc(vs_ok, 1)
                    dve.wait_ge(v_in, 32 * T + 32)
                    dve.tensor_copy(spare[:, :], eps[:, 0:1])

                def tile(T, t):
                    then, used = chain(dve, tile_ok, TILE * T)
                    tt, ts = dve.tensor_tensor, dve.tensor_scalar
                    ts(stage[:, 1, :].rearrange("p (a f) -> p a f", a=1),
                       omin[:, :].rearrange("p (a f) -> p a f", f=TP)[:, bass.ts(t, 1), :], 1.0, None, ALU.mult).then_inc(ost_ok, 1)
                    dve.wait_ge(om_ready, T + 1)
                    then(tt(oms[:, :], om_p[0:TP, 0:OMC], ombt[:, :], ALU.add))
                    then(tt(pos[:, :, :], base[:, :, :], oms[:, 0:2 * GK].rearrange("p (a k) -> p a k", a=2), ALU.add))
                    then(ts(pos[:, :, :], pos[:, :, :], -2.0, float(H + 1), ALU.max, ALU.min))
                    ts(base[:, 0, :], base[:, 0, :], 2.0, None, ALU.add)
                    then(dve.tensor_copy(whole[:, :, :], pos[:, :, :]))
                    then(dve.tensor_copy(low[:, :, :], whole[:, :, :]))
                    then(tt(over[:, :, :], low[:, :, :], pos[:, :, :], ALU.is_gt))
                    then(tt(low[:, :, :], low[:, :, :], over[:, :, :], ALU.subtract))
                    then(tt(frac[:, :, :], pos[:, :, :], low[:, :, :], ALU.subtract))
                    ts(rest[:, :, :], frac[:, :, :], -1.0, 1.0, ALU.mult, ALU.add)
                    then(ts(low[:, :, :], low[:, :, :], -2.0, float(H + 1), ALU.max, ALU.min))
                    tt(mk[:, 0, :], oms[:, 2 * GK:OMC], rest[:, 0, :], ALU.mult)
                    tt(mk[:, 1, :], oms[:, 2 * GK:OMC], frac[:, 0, :], ALU.mult)
                    then(ts(place[:, 0, :], low[:, 0, :], float(VP), None, ALU.mult))
                    for a in range(2):
                        tt(wt[:, 2 * a, :], mk[:, a, :], rest[:, 1, :], ALU.mult)
                        tt(wt[:, 2 * a + 1, :], mk[:, a, :], frac[:, 1, :], ALU.mult)
                    then(tt(place[:, 0, :], place[:, 0, :], low[:, 1, :], ALU.add))
                    then(tt(place[:, 0, :], place[:, 0, :], plc[:, 2, :], ALU.add))
                    for c, at in ((1, 1), (2, VP), (3, VP + 1)):
                        ins = ts(place[:, c, :], place[:, 0, :], float(at), None, ALU.add)
                    then(ins)
                    dve.tensor_copy(idx[:, :, :], place[:, :, :]).then_inc(idx_ok, 1)
                    dve.wait_ge(got_ok, T + 1)
                    then(tt(got[:, :, :, :], got[:, :, :, :], wt[:, :, :].unsqueeze(3).broadcast_to([TP, 4, GK, C // G]), ALU.mult))
                    dve.tensor_reduce(acc[:, :], got[:, :, :, :].rearrange("p a (k g) c -> p (g c) (a k)", g=G), AX.X,
                                      ALU.add).then_inc(acc_ok, 1)
                    dve.wait_ge(t_ready, T + 1)
                    dve.tensor_copy(acct[:, :], o_p[0:C, 0:TP]).then_inc(t_ok, 1)
                    dve.wait_ge(o_ready, T + 1)
                    yt = y[:, :].rearrange("p (a f) -> p a f", f=TP)[:, bass.ts(t, 1), :]
                    then(tt(yt, yt, st_p[0:C, 0:TP].rearrange("p (a f) -> p a f", a=1), ALU.add))
                    dve.tensor_copy(spare[:, :], y[:, 0:1]).then_inc(y_ok, 1)
                    assert used[0] == TILE, used

                far = dve.value_load(flag[0:1, 0:1], min_val=0, max_val=1)
                with dve.If(far > 0):
                    with dve.Fori(0, samples) as n:
                        x1_and_norm(n)
                        with dve.Fori(0, TILES) as t:
                            values(TILES * n + t, t)
                        with dve.Fori(0, TILES) as t:
                            tile(TILES * n + t, t)
                dve.wait_ge(ready, 1)

            @block.gpsimd
            def _(pool):
                far = pool.value_load(flag[0:1, 0:1], min_val=0, max_val=1)
                with pool.If(far > 0):
                    with pool.Fori(0, samples) as n:
                        then, used = chain(pool, pool_ok, 2 * n)
                        pool.wait_ge(var_ok, n + 1)
                        then(pool.tensor_tensor(gst[:, 2:3], gst[:, 1:2], eps[:, 0:1], ALU.add))
                        then(pool.tensor_tensor(gst[:, 2:3], gst[:, 2:3], eps[:, 1:2], ALU.pow))
                        pool.tensor_tensor(gst[:, 3:4], gst[:, 0:1], gst[:, 2:3], ALU.mult).then_inc(dev_ok, 1)
                        pool.wait_ge(v_in, 32 * TILES * (n + 1))
                        pool.sem_inc(carrier)
                        with pool.Fori(0, TILES) as t:
                            pool.wait_ge(idx_ok, TILES * n + t + 1)
                            pool.sem_inc(carrier)
                            for k in range(GK):
                                for c in range(4):
                                    pool.indirect_dma_start(out=got[:, c, k, :], out_offset=None, in_=vpad,
                                                            in_offset=bass.IndirectOffsetOnAxis(ap=idx[:, c, k:k + 1], axis=0)).then_inc(got_in, 16)
                            pool.wait_ge(got_in, 16 * 4 * GK)
                            pool.sem_inc(got_ok)
                            pool.inc_swdge_sem([got_in], [16 * 4 * GK], mode="sub")
                pool.wait_ge(ready, 1)

            @block.tensor
            def _(pe):
                far = pe.value_load(flag[0:1, 0:1], min_val=0, max_val=1)
                with pe.If(far > 0):
                    with pe.Fori(0, samples) as n:
                        pe.wait_ge(rh_ok, n + 1)
                        pe.matmul(st_p[:, 0:2], cst[0:C, 0, :], rh[:, :], start=True, stop=True).then_inc(st_ok, 1)
                        with pe.Fori(0, TILES) as t:
                            pe.wait_ge(vst_ok, TILES * n + t + 1)
                            pe.matmul(v_p[0:TP, 0:C], stage[:, 0, :], vpw, start=True, stop=True).then_inc(v_ready, 1)
                        with pe.Fori(0, TILES) as t:
                            T = TILES * n + t
                            pe.wait_ge(ost_ok, T + 1)
                            pe.matmul(om_p[0:TP, 0:OMC], stage[:, 1, :], omw, start=True, stop=True).then_inc(om_ready, 1)
                            pe.wait_ge(acc_ok, T + 1)
                            pe.matmul(o_p[0:C, 0:TP], acc[:, :], cst[0:TP, 1, 0:TP], start=True, stop=True).then_inc(t_ready, 1)
                            pe.wait_ge(t_ok, T + 1)
                            pe.matmul(st_p[:, 0:TP], opw, acct[:, :], start=True, stop=True).then_inc(o_ready, 1)
                pe.wait_ge(ready, 1)


def program(nc, x, w1t, w2t, par, con, con3, wts3, omb, vpb, places, out):
    samples = x.shape[0]
    pairs = samples // S
    l1_d = nc.dram_tensor("l1_scratch", [pairs, 128, HALF], f32).ap()
    l2_d = nc.dram_tensor("l2_scratch", [pairs, S * CO, HW], f32).ap()
    x3_d = nc.dram_tensor("x3_scratch", [samples, C, HW], f32).ap()
    vpad = nc.dram_tensor("value_scratch", [G * VP * VP, C // G], f32).ap()
    with nc.sbuf_tensor("ab3", [128, 2], f32) as ab3, nc.sbuf_tensor("flag", [1, 1], i32) as flag:
        l0_passes(nc, x, w1t, w2t, par, con, l1_d, l2_d, x3_d, ab3, pairs)
        l1_pass(nc, x, x3_d, l2_d, ab3, flag, con3, wts3, omb, vpb, out, pairs)
        l2_s = l2_d.rearrange("q (s c) f -> (q s) c f", s=S)
        general_pass(nc, x, x3_d, l2_s, ab3, flag, con3, wts3, omb, vpb, places, vpad, out, samples)


def kernel(x, L0_conv_w1, L0_conv_w2, L0_conv_g1, L0_conv_b1, L0_conv_g2, L0_conv_b2, L0_conv_g3, L0_conv_b3,
           L1_conv_dw_w, L1_conv_dw_b, L1_conv_om_w, L1_conv_om_b, L1_conv_vp_w, L1_conv_vp_b, L1_conv_op_w):
    import concourse.bacc as bacc
    from concourse.bass_utils import run_bass_kernel_spmd

    samples = x.shape[0]
    at = np.arange(128)

    par = np.zeros((128, 8), np.float32)
    for col, v in ((G1, L0_conv_g1), (B1, L0_conv_b1), (G2A, L0_conv_g2[:CO]), (G2B, L0_conv_g2[CO:]),
                   (B2A, L0_conv_b2[:CO]), (B2B, L0_conv_b2[CO:]), (G3, L0_conv_g3), (B3, L0_conv_b3)):
        par[:, col] = v[at % CO]

    h, s, o = at // 64, at // CO % S, at % CO
    con = np.zeros((128, 3, 128), np.float32)
    con[:, 0] = 0.25 * ((s[:, None] == s) & (o[:, None] // 4 == o // 4) & (o[:, None] % 2 == o % 2))
    con[:, 1] = 0.25 * (o[:, None] == o)
    con[:, 2] = (h[:, None] == 0) & (at // 64 == s[:, None]) & (at % 64 == o[:, None])

    om = L1_conv_om_w.reshape(G, 3 * TAPS, C)
    om_b = L1_conv_om_b.reshape(G, 3 * TAPS)
    yx = om[:, :2 * TAPS].reshape(G, TAPS, 2, C).transpose(2, 1, 0, 3).reshape(2 * GK, C)
    yx_b = om_b[:, :2 * TAPS].reshape(G, TAPS, 2).transpose(2, 1, 0).reshape(2 * GK)
    om = np.concatenate([yx, om[:, 2 * TAPS:].transpose(1, 0, 2).reshape(GK, C)], 0)
    om_b = np.concatenate([yx_b, om_b[:, 2 * TAPS:].T.reshape(GK)])
    wts3 = np.zeros((128, W3), np.float32)
    for s in range(S):
        r = slice(C * s, C * (s + 1))
        wts3[r, 0:OMC] = om.T
        wts3[r, OMC:OMC + C] = L1_conv_vp_w.T
        wts3[r, OMC + C * (1 + s):OMC + C * (2 + s)] = L1_conv_op_w.T
        wts3[r, OMC + 3 * C:OMC + 3 * C + TAPS] = L1_conv_dw_w.reshape(C, TAPS)
        wts3[r, W3 - 1] = L1_conv_dw_b
    con3 = np.zeros((128, 2, 128), np.float32)
    con3[:, 0, :] = 0.5 * (at[:, None] // 2 == at[None, :] // 2)
    con3[:, 1, :] = np.eye(128)

    lane, tap, group = np.arange(TP)[:, None], np.arange(GK) // G, np.arange(GK) % G
    places = np.zeros((TP, 3, GK), np.float32)
    places[:, 0] = lane // W + tap // 3 - 1
    places[:, 1] = lane % W + tap % 3 - 1
    places[:, 2] = group * VP * VP + 2 * VP + 2

    arrays = dict(
        x=x.reshape(samples, C, HW),
        w1t=L0_conv_w1.transpose(1, 2, 3, 0).reshape(CO, TAPS, CO),
        w2t=L0_conv_w2.transpose(1, 2, 3, 0).reshape(CO // 2, 2, TAPS, CO).transpose(1, 0, 2, 3),
        par=par, con=con, con3=con3, wts3=wts3,
        omb=np.tile(om_b[None], (LANES, 1)), vpb=np.tile(L1_conv_vp_b[None], (LANES, 1)), places=places)
    nc = bacc.Bacc("TRN2", target_bir_lowering=False, num_devices=1)
    args = []
    for name in arrays:
        arrays[name] = np.ascontiguousarray(arrays[name])
        args.append(nc.dram_tensor(name, arrays[name].shape, mybir.dt.from_np(arrays[name].dtype), kind="ExternalInput").ap())
    out = nc.dram_tensor("out", (samples, C, HW), f32, kind="ExternalOutput").ap()
    program(nc, *args, out)
    r = run_bass_kernel_spmd(nc, [arrays], core_ids=[0])
    return r.results[0]["out"].reshape(x.shape)
```
